# Optimizing a Trainium2 kernel written in Bass

```python
import numpy as np
import jax
import jax.numpy as jnp

def _softmax(x, axis=-1):
    return jax.nn.softmax(x, axis=axis)

def _gelu(x):
    return jax.nn.gelu(x, approximate=True)

def _silu(x):
    return jax.nn.silu(x)

def _sigmoid(x):
    return jax.nn.sigmoid(x)

def _layernorm(x, axis=-1, eps=1e-05):
    m = jnp.mean(x, axis=axis, keepdims=True)
    v = jnp.var(x, axis=axis, keepdims=True)
    return (x - m) / jnp.sqrt(v + eps)

def _scatter_add(tgt, idx, src, axis=0):
    return tgt.at[idx].add(src)

def _segment_sum(src, seg, n):
    return jax.ops.segment_sum(src, seg, n)
kernel_name = 'mk_rec_standalone_d1_rec_r8_3d522e'

def setup_inputs(seed: int=0):
    np.random.seed(seed)
    _w = jnp.asarray

    def _rec_inputs():
        import jax
        import jax.numpy as jnp
        _rk = jax.random.key(seed)
        r_user_ids = jax.random.randint(jax.random.fold_in(_rk, 1), (2048,), 79, 999919, jnp.int32)
        r_item_ids = jax.random.randint(jax.random.fold_in(_rk, 2), (2048,), 13, 999973, jnp.int32)
        r_sparse_features = jnp.stack([jax.random.randint(jax.random.fold_in(jax.random.fold_in(_rk, 3), 0), (2048,), 5, 99997, jnp.int32), jax.random.randint(jax.random.fold_in(jax.random.fold_in(_rk, 3), 1), (2048,), 10, 99989, jnp.int32), jax.random.randint(jax.random.fold_in(jax.random.fold_in(_rk, 3), 2), (2048,), 4, 99979, jnp.int32), jax.random.randint(jax.random.fold_in(jax.random.fold_in(_rk, 3), 3), (2048,), 11, 99996, jnp.int32), jax.random.randint(jax.random.fold_in(jax.random.fold_in(_rk, 3), 4), (2048,), 3, 12498, jnp.int32), jax.random.randint(jax.random.fold_in(jax.random.fold_in(_rk, 3), 5), (2048,), 3, 99999, jnp.int32), jax.random.randint(jax.random.fold_in(jax.random.fold_in(_rk, 3), 6), (2048,), 0, 99978, jnp.int32), jax.random.randint(jax.random.fold_in(jax.random.fold_in(_rk, 3), 7), (2048,), 1, 99980, jnp.int32), jax.random.randint(jax.random.fold_in(jax.random.fold_in(_rk, 3), 8), (2048,), 4, 99994, jnp.int32), jax.random.randint(jax.random.fold_in(jax.random.fold_in(_rk, 3), 9), (2048,), 16, 12500, jnp.int32), jax.random.randint(jax.random.fold_in(jax.random.fold_in(_rk, 3), 10), (2048,), 2, 99998, jnp.int32), jax.random.randint(jax.random.fold_in(jax.random.fold_in(_rk, 3), 11), (2048,), 1, 99985, jnp.int32), jax.random.randint(jax.random.fold_in(jax.random.fold_in(_rk, 3), 12), (2048,), 10, 99997, jnp.int32), jax.random.randint(jax.random.fold_in(jax.random.fold_in(_rk, 3), 13), (2048,), 3, 12500, jnp.int32), jax.random.randint(jax.random.fold_in(jax.random.fold_in(_rk, 3), 14), (2048,), 9, 99999, jnp.int32), jax.random.randint(jax.random.fold_in(jax.random.fold_in(_rk, 3), 15), (2048,), 4, 99999, jnp.int32), jax.random.randint(jax.random.fold_in(jax.random.fold_in(_rk, 3), 16), (2048,), 5, 99990, jnp.int32), jax.random.randint(jax.random.fold_in(jax.random.fold_in(_rk, 3), 17), (2048,), 0, 99998, jnp.int32), jax.random.randint(jax.random.fold_in(jax.random.fold_in(_rk, 3), 18), (2048,), 1, 99971, jnp.int32), jax.random.randint(jax.random.fold_in(jax.random.fold_in(_rk, 3), 19), (2048,), 9, 99997, jnp.int32), jax.random.randint(jax.random.fold_in(jax.random.fold_in(_rk, 3), 20), (2048,), 7, 99986, jnp.int32), jax.random.randint(jax.random.fold_in(jax.random.fold_in(_rk, 3), 21), (2048,), 13, 99998, jnp.int32), jax.random.randint(jax.random.fold_in(jax.random.fold_in(_rk, 3), 22), (2048,), 3, 99999, jnp.int32), jax.random.randint(jax.random.fold_in(jax.random.fold_in(_rk, 3), 23), (2048,), 7, 12500, jnp.int32), jax.random.randint(jax.random.fold_in(jax.random.fold_in(_rk, 3), 24), (2048,), 1, 99994, jnp.int32), jax.random.randint(jax.random.fold_in(jax.random.fold_in(_rk, 3), 25), (2048,), 0, 12500, jnp.int32)], axis=1)
        return (r_user_ids, r_item_ids, r_sparse_features)
    r_user_ids, r_item_ids, r_sparse_features = _rec_inputs()

    def _L0_rec_setup():
        import jax, jax.numpy as jnp
        import numpy as np
        B = 2048
        NUM_SPARSE = 26
        EMB = 64
        USER_VOCAB = 125000
        ITEM_VOCAB = 125000
        SPARSE_VOCAB = 12500
        HIDDEN = 2 * EMB
        MLP_IN = EMB * (NUM_SPARSE + 2)
        key = jax.random.key(seed)
        ks = jax.random.split(key, 10)
        s = 0.05
        return {'user_ids': jax.random.randint(ks[0], (B,), 0, USER_VOCAB), 'item_ids': jax.random.randint(ks[1], (B,), 0, ITEM_VOCAB), 'sparse_features': jax.random.randint(ks[2], (B, NUM_SPARSE), 0, SPARSE_VOCAB), 'user_emb': jax.random.normal(ks[3], (USER_VOCAB, EMB), jnp.float32) * s, 'item_emb': jax.random.normal(ks[4], (ITEM_VOCAB, EMB), jnp.float32) * s, 'sparse_tables': jax.random.normal(ks[5], (NUM_SPARSE, SPARSE_VOCAB, EMB), jnp.float32) * s, 'W1': jax.random.normal(ks[6], (MLP_IN, HIDDEN), jnp.float32) * (1.0 / np.sqrt(MLP_IN)), 'b1': jnp.zeros((HIDDEN,), jnp.float32), 'W2': jax.random.normal(ks[7], (HIDDEN, 1), jnp.float32) * (1.0 / np.sqrt(HIDDEN)), 'b2': jnp.zeros((1,), jnp.float32)}
    _L0_rec_all = _L0_rec_setup()
    _L0_rec_in = {k: v for k, v in _L0_rec_all.items() if k in ('user_emb', 'item_emb', 'sparse_tables', 'W1', 'b1', 'W2', 'b2')}
    del _L0_rec_all
    return {'r_user_ids': r_user_ids, 'r_item_ids': r_item_ids, 'r_sparse_features': r_sparse_features, 'L0_rec_user_emb': _L0_rec_in['user_emb'], 'L0_rec_item_emb': _L0_rec_in['item_emb'], 'L0_rec_sparse_tables': _L0_rec_in['sparse_tables'], 'L0_rec_W1': _L0_rec_in['W1'], 'L0_rec_b1': _L0_rec_in['b1'], 'L0_rec_W2': _L0_rec_in['W2'], 'L0_rec_b2': _L0_rec_in['b2']}

def reference(r_user_ids, r_item_ids, r_sparse_features, L0_rec_user_emb, L0_rec_item_emb, L0_rec_sparse_tables, L0_rec_W1, L0_rec_b1, L0_rec_W2, L0_rec_b2):
    import jax
    import jax.numpy as jnp

    def _L0_rec_ref(user_ids, item_ids, sparse_features, user_emb, item_emb, sparse_tables, W1, b1, W2, b2):
        import jax, jax.numpy as jnp
        import numpy as np
        B = 2048
        NUM_SPARSE = 26
        EMB = 64
        USER_VOCAB = 125000
        ITEM_VOCAB = 125000
        SPARSE_VOCAB = 12500
        HIDDEN = 2 * EMB
        MLP_IN = EMB * (NUM_SPARSE + 2)
        ue = user_emb[user_ids]
        ie = item_emb[item_ids]
        se = jax.vmap(lambda t, idx: t[idx], in_axes=(0, 1), out_axes=1)(sparse_tables, sparse_features)
        se = se.reshape(se.shape[0], -1)
        concat = jnp.concatenate([ue, ie, se], axis=-1)
        h = jax.nn.relu(concat @ W1 + b1)
        raw = h @ W2 + b2
        return jax.nn.sigmoid(raw)
    y = _L0_rec_ref(r_user_ids, r_item_ids, r_sparse_features, L0_rec_user_emb, L0_rec_item_emb, L0_rec_sparse_tables, L0_rec_W1, L0_rec_b1, L0_rec_W2, L0_rec_b2)
    return y

_drawn_inputs = setup_inputs


def setup_inputs(seed=0):
    import zlib

    import numpy as np

    out = dict(_drawn_inputs(seed))
    spreads = {'L0_rec_b1': (0.0, 0.1)}
    factors = {'L0_rec_user_emb': 8.0,
     'L0_rec_item_emb': 8.0,
     'L0_rec_sparse_tables': 4.27,
     'L0_rec_W1': 4.431,
     'L0_rec_W2': 4.75}
    for name, (base, spread) in spreads.items():
        noise = np.random.default_rng([zlib.crc32(name.encode()), seed]).standard_normal(out[name].shape)
        drawn = base * np.exp(spread * noise) if base else spread * noise
        out[name] = jnp.asarray(drawn.astype(out[name].dtype))
    for name, factor in factors.items():
        out[name] = (out[name] * factor).astype(out[name].dtype)
    return out
```

```python
from contextlib import ExitStack

import concourse.bass as bass
from concourse import mybir

ALU = mybir.AluOpType
ACT = mybir.ActivationFunctionType
F32 = mybir.dt.float32
I32 = mybir.dt.int32
U32 = mybir.dt.uint32

P = 128
SLOTS = 2
AHEAD = 2
DMA_INC = 16
GROUPS = [(0, 4), (4, 8), (8, 12), (12, 13), (13, 14)]


def rec_mlp(nc, user_ids, item_ids, sparse_ids, user_emb, item_emb, sparse_tables, W1, b1, W2, b2, ident, out):
    B = user_ids.shape[0]
    fields = sparse_ids.shape[1]
    vocab, emb = user_emb.shape
    sparse_vocab = sparse_tables.shape[1]
    features, hidden = W1.shape
    tiles = B // P
    steps = tiles // SLOTS
    chunks = features // P
    per_chunk = P // emb
    assert item_emb.shape == user_emb.shape and features == (fields + 2) * emb
    assert tiles * P == B and steps * SLOTS == tiles and GROUPS[-1][1] == chunks and hidden == P

    sparse_rows = sparse_tables.rearrange("f v e -> (f v) e")
    widest = max(b - a for a, b in GROUPS)

    with ExitStack() as ctx:
        def sb(name, shape, dt=F32):
            return ctx.enter_context(nc.sbuf_tensor(name, shape, dt))

        def psum(name, shape):
            return ctx.enter_context(nc.psum_tensor(name, shape, F32))

        def sem(name):
            return ctx.enter_context(nc.semaphore(name))

        pair_ids = sb("pair_ids", [P, 2, tiles], I32)
        pair_wrap = sb("pair_wrap", [P, 2, tiles])
        field_ids = sb("field_ids", [P, tiles, fields], I32)
        field_wrap = sb("field_wrap", [P, tiles, fields])
        all_rows = sb("all_rows", [P, tiles, fields + 2], U32)
        rows = [sb(f"rows{s}", [P, fields + 2], U32) for s in range(SLOTS)]
        w1 = sb("w1", [P, chunks, hidden])
        b1_row = sb("b1_row", [1, hidden])
        ones_row = sb("ones_row", [1, P])
        w2_all = sb("w2_all", [P, hidden])
        b2_all = sb("b2_all", [P, 1])
        eye = sb("eye", [P, P])
        x = [sb(f"x{s}", [P, features]) for s in range(SLOTS)]
        xt = [sb(f"xt{k}", [P, widest * P]) for k in range(2)]
        weighed = sb("weighed", [P, hidden])
        raw = sb("raw", [P, tiles])
        y = sb("y", [P, tiles])

        xt_ps = [psum(f"xt_ps{k}", [P, widest * P]) for k in range(2)]
        h_ps = [psum(f"h_ps{s}", [P, 512]) for s in range(SLOTS)]

        pair_loaded = sem("pair_loaded")
        fields_loaded = sem("fields_loaded")
        index_step = sem("index_step")
        all_rows_ready = sem("all_rows_ready")
        rows_ready = sem("rows_ready")
        weights_loaded = sem("weights_loaded")
        head_loaded = sem("head_loaded")
        ones_ready = sem("ones_ready")
        gathered = [[sem(f"gathered_{s}_{g}") for g in range(len(GROUPS))] for s in range(SLOTS)]
        turned = sem("turned")
        moved = sem("moved")
        multiplied = sem("multiplied")
        raw_ready = sem("raw_ready")
        y_ready = sem("y_ready")
        stored = sem("stored")

        block = ctx.enter_context(nc.Block())
        NG = len(GROUPS)
        STEP_GROUPS = SLOTS * NG

        @block.sync
        def _(sp):
            sp.dma_start(pair_ids[:, 0, :], user_ids.rearrange("(p t) -> p t", p=P)).then_inc(pair_loaded, DMA_INC)
            sp.dma_start(pair_ids[:, 1, :], item_ids.rearrange("(p t) -> p t", p=P)).then_inc(pair_loaded, DMA_INC)
            sp.dma_start(eye[:], ident).then_inc(weights_loaded, DMA_INC)
            sp.dma_start(b1_row[:], b1.rearrange("(a n) -> a n", a=1)).then_inc(weights_loaded, DMA_INC)
            sp.dma_start(w1[:], W1.rearrange("(c p) n -> p c n", p=P)).then_inc(weights_loaded, DMA_INC)
            sp.dma_start(w2_all[:], W2.rearrange("n a -> a n").broadcast_to([P, hidden])).then_inc(head_loaded, DMA_INC)
            sp.dma_start(b2_all[:], b2.rearrange("(a n) -> a n", a=1).broadcast_to([P, 1])).then_inc(head_loaded, DMA_INC)
            sp.wait_ge(y_ready, 1)
            sp.dma_start(out.rearrange("(p t) a -> p (t a)", p=P), y[:]).then_inc(stored, DMA_INC)
            sp.wait_ge(stored, DMA_INC)

        @block.gpsimd
        def _(pool):
            with pool.Fori(0, steps) as i:
                for s in range(SLOTS):
                    pool.wait_ge(rows_ready, i * SLOTS + (s + 1))
                    pool.nop(nofuse=True)
                    for g, (first, last) in enumerate(GROUPS):
                        for f in range(first * per_chunk, last * per_chunk):
                            table = (user_emb, item_emb)[f] if f < 2 else sparse_rows
                            nc.gpsimd.indirect_dma_start(
                                out=x[s][:, f * emb:(f + 1) * emb], out_offset=None, in_=table,
                                in_offset=bass.IndirectOffsetOnAxis(ap=rows[s][:, f:f + 1], axis=0),
                                element_offset=max(f - 2, 0) * sparse_vocab * emb,
                            ).then_inc(gathered[s][g], DMA_INC)

        @block.vector
        def _(dve):
            def table_rows(n, ids, wrap, to, size, loaded, arrived):
                dve.wait_ge(loaded, arrived)
                nc.vector.tensor_scalar(wrap[:], ids[:], 0.0, float(size), ALU.is_lt, ALU.mult).then_inc(index_step, 1)
                dve.wait_ge(index_step, 2 * n + 1)
                nc.vector.tensor_tensor(wrap[:], wrap[:], ids[:], ALU.add).then_inc(index_step, 1)
                dve.wait_ge(index_step, 2 * n + 2)
                nc.vector.tensor_scalar(to, wrap[:], 0.0, float(size - 1), ALU.max, ALU.min).then_inc(all_rows_ready, 1)

            def slot_rows(s, tile):
                nc.vector.tensor_copy(rows[s][:, None, :], all_rows[:, tile, :]).then_inc(rows_ready, 1)

            def head(s, i):
                dve.wait_ge(multiplied, i * STEP_GROUPS + ((s + 1) * NG + AHEAD))
                dve.wait_ge(raw_ready, i * SLOTS + (s + AHEAD))
                nc.vector.scalar_tensor_tensor(
                    out=weighed[:], in0=h_ps[s][:, :hidden], scalar=0.0, in1=w2_all[:], op0=ALU.max,
                    op1=ALU.mult, accum_out=raw[:, bass.ds(i * SLOTS + s, 1)]).then_inc(raw_ready, 1)

            table_rows(0, pair_ids, pair_wrap, all_rows[:, :, 0:2].rearrange("p t f -> p f t"), vocab,
                       pair_loaded, 2 * DMA_INC)
            table_rows(1, field_ids, field_wrap, all_rows[:, :, 2:], sparse_vocab, fields_loaded, DMA_INC)
            dve.wait_ge(all_rows_ready, 2)
            for s in range(SLOTS):
                slot_rows(s, bass.ds(s, 1))
            nc.vector.memset(ones_row[:], 1.0).then_inc(ones_ready, 1)
            dve.sem_inc(raw_ready, AHEAD)
            dve.wait_ge(head_loaded, 2 * DMA_INC)
            with dve.Fori(0, steps - 1) as i:
                for s in range(SLOTS):
                    dve.wait_ge(turned, i * STEP_GROUPS + (s + 1) * NG)
                    slot_rows(s, bass.ds(i * SLOTS + (SLOTS + s), 1))
                    head(s, i)
            for s in range(SLOTS):
                head(s, steps - 1)

        @block.scalar
        def _(act):
            act.dma_start(field_ids[:].rearrange("p t f -> p (t f)"),
                          sparse_ids.rearrange("(p t) f -> p (t f)", p=P)).then_inc(fields_loaded, DMA_INC)
            with act.Fori(0, steps) as i:
                for s in range(SLOTS):
                    for g, (first, last) in enumerate(GROUPS):
                        n = s * NG + g
                        width = (last - first) * P
                        act.wait_ge(turned, i * STEP_GROUPS + (n + 1))
                        act.wait_ge(multiplied, i * STEP_GROUPS + (n + 1))
                        nc.scalar.copy(xt[n % 2][:, :width], xt_ps[n % 2][:, :width]).then_inc(moved, 1)
            act.wait_ge(head_loaded, 2 * DMA_INC)
            act.wait_ge(raw_ready, tiles + AHEAD)
            nc.scalar.activation(y[:], raw[:], ACT.Sigmoid, bias=b2_all[:, 0:1]).then_inc(y_ready, 1)

        @block.tensor
        def _(pe):
            pe.wait_ge(weights_loaded, 3 * DMA_INC)
            pe.wait_ge(ones_ready, 1)
            pe.sem_inc(multiplied, AHEAD)
            with pe.Fori(0, steps) as i:
                for s in range(SLOTS):
                    pe.wait_ge(raw_ready, i * SLOTS + (s + 1))
                    nc.tensor.matmul(h_ps[s][:, :hidden], ones_row[:], b1_row[:], start=True, stop=False)
                    for g, (first, last) in enumerate(GROUPS):
                        n = s * NG + g
                        count = (last - first) * per_chunk
                        pe.wait_ge(gathered[s][g], i * (count * DMA_INC) + count * DMA_INC)
                        for c in range(first, last):
                            mm = nc.tensor.transpose(xt_ps[n % 2][:, (c - first) * P:(c - first + 1) * P],
                                                     x[s][:, c * P:(c + 1) * P], eye[:])
                        mm.then_inc(turned, 1)
                        pe.wait_ge(moved, i * STEP_GROUPS + (n + 1))
                        for c in range(first, last):
                            mm = nc.tensor.matmul(h_ps[s][:, :hidden], xt[n % 2][:, (c - first) * P:(c - first + 1) * P],
                                                  w1[:, c, :], start=False, stop=(c == chunks - 1))
                        mm.then_inc(multiplied, 1)


_INS = ['r_user_ids', 'r_item_ids', 'r_sparse_features', 'L0_rec_user_emb', 'L0_rec_item_emb',
        'L0_rec_sparse_tables', 'L0_rec_W1', 'L0_rec_b1', 'L0_rec_W2', 'L0_rec_b2']


def kernel(**inputs):
    import numpy as _np
    import concourse.bacc as _bacc
    from concourse import mybir as _mybir
    from concourse.bass_utils import run_bass_kernel_spmd as _run

    nc = _bacc.Bacc("TRN2", target_bir_lowering=False, num_devices=1)
    arrays, args = {}, []
    for name in _INS:
        a = _np.ascontiguousarray(inputs[name])
        arrays[f"in_{name}_dram"] = a
        args.append(nc.dram_tensor(f"in_{name}_dram", a.shape, _mybir.dt.from_np(a.dtype), kind="ExternalInput").ap())
    eye = _np.eye(128, dtype=_np.float32)
    arrays["eye_dram"] = eye
    args.append(nc.dram_tensor("eye_dram", eye.shape, _mybir.dt.float32, kind="ExternalInput").ap())
    args.append(nc.dram_tensor("out_dram", (2048, 1), _mybir.dt.float32, kind="ExternalOutput").ap())
    rec_mlp(nc, *args)
    r = _run(nc, [arrays], core_ids=[0])
    return r.results[0]["out_dram"]
```

```python
from contextlib import ExitStack

import concourse.bass as bass
from concourse import mybir

ALU = mybir.AluOpType
ACT = mybir.ActivationFunctionType
F32 = mybir.dt.float32
I32 = mybir.dt.int32
U32 = mybir.dt.uint32

P = 128
SLOTS = 2
AHEAD = 2
DMA_INC = 16
GROUPS = [(0, 4), (4, 8), (8, 12), (12, 13), (13, 14)]


def rec_mlp(nc, user_ids, item_ids, sparse_ids, user_emb, item_emb, sparse_tables, W1, b1, W2, b2, ident, out):
    B = user_ids.shape[0]
    fields = sparse_ids.shape[1]
    vocab, emb = user_emb.shape
    sparse_vocab = sparse_tables.shape[1]
    features, hidden = W1.shape
    tiles = B // P
    steps = tiles // SLOTS
    chunks = features // P
    per_chunk = P // emb
    assert item_emb.shape == user_emb.shape and features == (fields + 2) * emb
    assert tiles * P == B and steps * SLOTS == tiles and GROUPS[-1][1] == chunks and hidden == P

    sparse_rows = sparse_tables.rearrange("f v e -> (f v) e")
    widest = max(b - a for a, b in GROUPS)

    with ExitStack() as ctx:
        def sb(name, shape, dt=F32):
            return ctx.enter_context(nc.sbuf_tensor(name, shape, dt))

        def psum(name, shape):
            return ctx.enter_context(nc.psum_tensor(name, shape, F32))

        def sem(name):
            return ctx.enter_context(nc.semaphore(name))

        pair_ids = sb("pair_ids", [P, 2, tiles], I32)
        field_ids = sb("field_ids", [P, tiles, fields], I32)
        wrap = sb("wrap", [P, fields + 2])
        rows = [sb(f"rows{s}", [P, fields + 2], U32) for s in range(SLOTS)]
        warm = sb("warm", [1, 1])
        w1 = sb("w1", [P, chunks, hidden])
        b1_row = sb("b1_row", [1, hidden])
        ones_row = sb("ones_row", [1, P])
        w2_all = sb("w2_all", [P, hidden])
        b2_all = sb("b2_all", [P, 1])
        eye = sb("eye", [P, P])
        x = [sb(f"x{s}", [P, features]) for s in range(SLOTS)]
        xt = [sb(f"xt{k}", [P, widest * P]) for k in range(2)]
        weighed = sb("weighed", [P, hidden])
        raw = sb("raw", [P, tiles])
        y = sb("y", [P, tiles])

        xt_ps = [psum(f"xt_ps{k}", [P, widest * P]) for k in range(2)]
        h_ps = [psum(f"h_ps{s}", [P, 512]) for s in range(SLOTS)]

        pair_loaded = sem("pair_loaded")
        fields_loaded = sem("fields_loaded")
        index_step = sem("index_step")
        rows_ready = sem("rows_ready")
        weights_loaded = sem("weights_loaded")
        head_loaded = sem("head_loaded")
        ones_ready = sem("ones_ready")
        gathered = [[sem(f"gathered_{s}_{g}") for g in range(len(GROUPS))] for s in range(SLOTS)]
        turned = sem("turned")
        moved = sem("moved")
        multiplied = sem("multiplied")
        raw_ready = sem("raw_ready")
        y_ready = sem("y_ready")
        stored = sem("stored")

        block = ctx.enter_context(nc.Block())
        NG = len(GROUPS)
        STEP_GROUPS = SLOTS * NG

        @block.sync
        def _(sp):
            sp.dma_start(pair_ids[:, 0, :], user_ids.rearrange("(p t) -> p t", p=P)).then_inc(pair_loaded, DMA_INC)
            sp.dma_start(eye[:], ident).then_inc(weights_loaded, DMA_INC)
            sp.dma_start(b1_row[:], b1.rearrange("(a n) -> a n", a=1)).then_inc(weights_loaded, DMA_INC)
            sp.dma_start(w1[:], W1.rearrange("(c p) n -> p c n", p=P)).then_inc(weights_loaded, DMA_INC)
            sp.dma_start(w2_all[:], W2.rearrange("n a -> a n").broadcast_to([P, hidden])).then_inc(head_loaded, DMA_INC)
            sp.dma_start(b2_all[:], b2.rearrange("(a n) -> a n", a=1).broadcast_to([P, 1])).then_inc(head_loaded, DMA_INC)
            sp.wait_ge(y_ready, 1)
            sp.dma_start(out.rearrange("(p t) a -> p (t a)", p=P), y[:]).then_inc(stored, DMA_INC)
            sp.wait_ge(stored, DMA_INC)

        @block.gpsimd
        def _(pool):
            with pool.Fori(0, steps) as i:
                for s in range(SLOTS):
                    for g, (first, last) in enumerate(GROUPS):
                        for f in range(first * per_chunk, last * per_chunk):
                            if f in (0, 2):
                                pool.wait_ge(rows_ready, i * (2 * SLOTS) + (2 * s + 1 + f // 2))
                                pool.nop(nofuse=True)
                            table = (user_emb, item_emb)[f] if f < 2 else sparse_rows
                            nc.gpsimd.indirect_dma_start(
                                out=x[s][:, f * emb:(f + 1) * emb], out_offset=None, in_=table,
                                in_offset=bass.IndirectOffsetOnAxis(ap=rows[s][:, f:f + 1], axis=0),
                                element_offset=max(f - 2, 0) * sparse_vocab * emb,
                            ).then_inc(gathered[s][g], DMA_INC)

        @block.vector
        def _(dve):
            def table_rows(n, ids, size, first, last, s):
                w, r = wrap[:, first:last], rows[s][:, first:last]
                if first:
                    dve.wait_ge(rows_ready, n)
                nc.vector.tensor_scalar(w, ids, 0.0, float(size), ALU.is_lt, ALU.mult).then_inc(index_step, 1)
                dve.wait_ge(index_step, n * 2 + 1)
                nc.vector.tensor_tensor(w, w, ids, ALU.add).then_inc(index_step, 1)
                dve.wait_ge(index_step, n * 2 + 2)
                nc.vector.tensor_scalar(r, w, 0.0, float(size - 1), ALU.max, ALU.min).then_inc(rows_ready, 1)

            def pair_table_rows(tile, s):
                table_rows(tile * 2, pair_ids[:, :, bass.ds(tile, 1)].rearrange("p f t -> p (f t)"), vocab, 0, 2, s)

            def field_table_rows(tile, s):
                table_rows(tile * 2 + 1, field_ids[:, bass.ds(tile, 1), :].rearrange("p t f -> p (t f)"),
                           sparse_vocab, 2, fields + 2, s)

            def head(s, i):
                dve.wait_ge(multiplied, i * STEP_GROUPS + ((s + 1) * NG + AHEAD))
                dve.wait_ge(raw_ready, i * SLOTS + (s + AHEAD))
                nc.vector.scalar_tensor_tensor(
                    out=weighed[:], in0=h_ps[s][:, :hidden], scalar=0.0, in1=w2_all[:], op0=ALU.max,
                    op1=ALU.mult, accum_out=raw[:, bass.ds(i * SLOTS + s, 1)]).then_inc(raw_ready, 1)

            dve.wait_ge(pair_loaded, 2 * DMA_INC)
            pair_table_rows(0, 0)
            dve.wait_ge(fields_loaded, DMA_INC)
            field_table_rows(0, 0)
            for s in range(1, SLOTS):
                pair_table_rows(s, s)
                field_table_rows(s, s)
            nc.vector.memset(ones_row[:], 1.0).then_inc(ones_ready, 1)
            dve.sem_inc(raw_ready, AHEAD)
            dve.wait_ge(head_loaded, 2 * DMA_INC)
            with dve.Fori(0, steps - 1) as i:
                for s in range(SLOTS):
                    dve.wait_ge(turned, i * STEP_GROUPS + (s + 1) * NG)
                    pair_table_rows(i * SLOTS + (SLOTS + s), s)
                    field_table_rows(i * SLOTS + (SLOTS + s), s)
                    head(s, i)
            for s in range(SLOTS):
                head(s, steps - 1)

        @block.scalar
        def _(act):
            act.dma_start(pair_ids[:, 1, :], item_ids.rearrange("(p t) -> p t", p=P)).then_inc(pair_loaded, DMA_INC)
            act.dma_start(field_ids[:].rearrange("p t f -> p (t f)"),
                          sparse_ids.rearrange("(p t) f -> p (t f)", p=P)).then_inc(fields_loaded, DMA_INC)
            nc.scalar.activation(warm[:], nc.const_aps.tensor(0.0, (1, 1), F32), ACT.Sigmoid)
            with act.Fori(0, steps) as i:
                for s in range(SLOTS):
                    for g, (first, last) in enumerate(GROUPS):
                        n = s * NG + g
                        width = (last - first) * P
                        act.wait_ge(turned, i * STEP_GROUPS + (n + 1))
                        act.wait_ge(multiplied, i * STEP_GROUPS + (n + 1))
                        nc.scalar.copy(xt[n % 2][:, :width], xt_ps[n % 2][:, :width]).then_inc(moved, 1)
            act.wait_ge(head_loaded, 2 * DMA_INC)
            act.wait_ge(raw_ready, tiles + AHEAD)
            nc.scalar.activation(y[:], raw[:], ACT.Sigmoid, bias=b2_all[:, 0:1]).then_inc(y_ready, 1)

        @block.tensor
        def _(pe):
            pe.wait_ge(weights_loaded, 3 * DMA_INC)
            pe.wait_ge(ones_ready, 1)
            pe.sem_inc(multiplied, AHEAD)
            with pe.Fori(0, steps) as i:
                for s in range(SLOTS):
                    pe.wait_ge(raw_ready, i * SLOTS + (s + 1))
                    nc.tensor.matmul(h_ps[s][:, :hidden], ones_row[:], b1_row[:], start=True, stop=False)
                    for g, (first, last) in enumerate(GROUPS):
                        n = s * NG + g
                        count = (last - first) * per_chunk
                        pe.wait_ge(gathered[s][g], i * (count * DMA_INC) + count * DMA_INC)
                        for c in range(first, last):
                            mm = nc.tensor.transpose(xt_ps[n % 2][:, (c - first) * P:(c - first + 1) * P],
                                                     x[s][:, c * P:(c + 1) * P], eye[:])
                        mm.then_inc(turned, 1)
                        pe.wait_ge(moved, i * STEP_GROUPS + (n + 1))
                        for c in range(first, last):
                            mm = nc.tensor.matmul(h_ps[s][:, :hidden], xt[n % 2][:, (c - first) * P:(c - first + 1) * P],
                                                  w1[:, c, :], start=False, stop=(c == chunks - 1))
                        mm.then_inc(multiplied, 1)


_INS = ['r_user_ids', 'r_item_ids', 'r_sparse_features', 'L0_rec_user_emb', 'L0_rec_item_emb',
        'L0_rec_sparse_tables', 'L0_rec_W1', 'L0_rec_b1', 'L0_rec_W2', 'L0_rec_b2']


def kernel(**inputs):
    import numpy as _np
    import concourse.bacc as _bacc
    from concourse import mybir as _mybir
    from concourse.bass_utils import run_bass_kernel_spmd as _run

    nc = _bacc.Bacc("TRN2", target_bir_lowering=False, num_devices=1)
    arrays, args = {}, []
    for name in _INS:
        a = _np.ascontiguousarray(inputs[name])
        arrays[f"in_{name}_dram"] = a
        args.append(nc.dram_tensor(f"in_{name}_dram", a.shape, _mybir.dt.from_np(a.dtype), kind="ExternalInput").ap())
    eye = _np.eye(128, dtype=_np.float32)
    arrays["eye_dram"] = eye
    args.append(nc.dram_tensor("eye_dram", eye.shape, _mybir.dt.float32, kind="ExternalInput").ap())
    args.append(nc.dram_tensor("out_dram", (2048, 1), _mybir.dt.float32, kind="ExternalOutput").ap())
    rec_mlp(nc, *args)
    r = _run(nc, [arrays], core_ids=[0])
    return r.results[0]["out_dram"]
```

```python
from contextlib import ExitStack

import concourse.bass as bass
from concourse import mybir

ALU = mybir.AluOpType
ACT = mybir.ActivationFunctionType
F32 = mybir.dt.float32
BF16 = mybir.dt.bfloat16
I32 = mybir.dt.int32
U32 = mybir.dt.uint32

P = 128
SLOTS = 2
AHEAD = 2
DMA_INC = 16
GATHERED = [(0, 4), (4, 8), (8, 12), (12, 13)]
FULL = GATHERED + [(13, 14)]
FIRST_SCANNED = 2
SCANNED = 2
BLOCKS = [(0, 0), (0, 1), (1, 0)]
REACH = 100
MASKS = 10
AT_ONCE = 5
PIECE = 5
LOADED = 2
SPREAD = 112


def rec_mlp(nc, user_ids, item_ids, sparse_ids, user_emb, item_emb, sparse_tables, W1, b1, W2, b2,
            scan_order_ids, ident, scan_numbers, out):
    B = user_ids.shape[0]
    fields = sparse_ids.shape[1]
    vocab, emb = user_emb.shape
    sparse_vocab = sparse_tables.shape[1]
    features, hidden = W1.shape
    tiles = B // P
    steps = tiles // SLOTS
    chunks = features // P
    per_chunk = P // emb
    first_scanned_field = fields - SCANNED
    holders = sparse_vocab // REACH
    scans = steps - FIRST_SCANNED
    width = len(BLOCKS) * P
    table_cols = [(P * BLOCKS.index((a, 0)), P * sum(t == a for t, _ in BLOCKS)) for a in range(SCANNED)]
    block_cols = [[(a, P * n) for n, (a, slot) in enumerate(BLOCKS) if slot == s] for s in range(SLOTS)]
    rounds = REACH // MASKS
    pieces = SCANNED * REACH // PIECE
    loads = pieces // LOADED
    cols = PIECE * emb
    later_tiles = tiles - SLOTS
    assert item_emb.shape == user_emb.shape and features == (fields + 2) * emb
    assert tiles * P == B and steps * SLOTS == tiles and hidden == P and SCANNED == per_chunk == 2
    assert GATHERED[-1][1] == chunks - 1 and FULL[-1][1] == chunks
    assert holders * REACH == sparse_vocab and holders <= P and rounds * MASKS == REACH <= 256

    sparse_rows = sparse_tables.rearrange("f v e -> (f v) e")
    widest = max(b - a for a, b in FULL)

    def groups_of(i):
        return FULL if isinstance(i, int) and i < FIRST_SCANNED else GATHERED

    def half(i, s):
        return groups_of(i) is GATHERED and (SCANNED - 1, s) not in BLOCKS

    def group_base(i):
        if isinstance(i, int) and i < FIRST_SCANNED:
            return i * (SLOTS * len(FULL))
        return i * (SLOTS * len(GATHERED)) + FIRST_SCANNED * SLOTS * (len(FULL) - len(GATHERED))

    def rounds_after(i):
        tile = [1, 1, 1, 1, 1] if groups_of(i) is FULL else [2, 1, 1, 1]
        assert SLOTS * sum(tile) == rounds
        return tile

    with ExitStack() as ctx:
        def sb(name, shape, dt=F32):
            return ctx.enter_context(nc.sbuf_tensor(name, shape, dt))

        def psum(name, shape):
            return ctx.enter_context(nc.psum_tensor(name, shape, F32))

        def sem(name):
            return ctx.enter_context(nc.semaphore(name))

        pair_ids = sb("pair_ids", [P, 2, tiles], I32)
        field_ids = sb("field_ids", [P, tiles, fields], I32)
        scan_ids = sb("scan_ids", [1, scans * width], I32)
        scan_ids_f = sb("scan_ids_f", [1, scans * width])
        wrap = sb("wrap", [P, fields + 2])
        wrap_later = sb("wrap_later", [P, later_tiles, fields + 2])
        later_rows = sb("later_rows", [P, later_tiles, fields + 2])
        rows = [sb(f"rows{s}", [P, fields + 2], U32) for s in range(SLOTS)]
        warm = sb("warm", [1, 1])
        w1 = sb("w1", [P, chunks, hidden])
        w1_scan = sb("w1_scan", [P, SCANNED, hidden])
        b1_row = sb("b1_row", [1, hidden])
        ones_row = sb("ones_row", [1, P])
        w2_all = sb("w2_all", [P, hidden])
        b2_all = sb("b2_all", [P, 1])
        eye = sb("eye", [P, P])
        numbers = sb("numbers", [P, REACH + 1])
        x = [sb(f"x{s}", [P, features]) for s in range(SLOTS)]
        xt = [sb(f"xt{k}", [P, widest * P]) for k in range(2)]
        weighed = sb("weighed", [P, hidden])
        raw = sb("raw", [P, tiles])
        y = sb("y", [P, tiles])
        loaded_rows = [sb(f"loaded_rows{k}", [holders, LOADED * cols]) for k in range(2)]
        high_mid = sb("high_mid", [holders, SCANNED * REACH, 2 * emb], BF16)
        low = sb("low", [holders, SCANNED * REACH, 2 * emb], BF16)
        zeros = sb("zeros", [holders, width], BF16)
        wanted = sb("wanted", [holders, width])
        reach_of = sb("reach_of", [holders, width], BF16)
        mask = [sb(f"mask{k}", [holders, width], BF16) for k in range(MASKS)]
        picked = sb("picked", [P, width])

        xt_ps = [psum(f"xt_ps{k}", [P, widest * P]) for k in range(2)]
        h_ps = [psum(f"h_ps{s}", [P, 512]) for s in range(SLOTS)]
        split_ps = [psum(f"split_ps{k}", [P, 512]) for k in range(2)]
        spread_ps = split_ps[0]
        reach_of_ps = psum("reach_of_ps", [P, 512])
        picked_ps = psum("picked_ps", [P, 512])
        reach_words = reach_of_ps.bitcast(U32)[:holders, :width // 2]
        reach_ps = reach_of_ps.bitcast(BF16)[:holders, :width]

        pair_loaded = sem("pair_loaded")
        fields_loaded = sem("fields_loaded")
        scan_ids_loaded = sem("scan_ids_loaded")
        scan_ids_ready = sem("scan_ids_ready")
        index_step = sem("index_step")
        rows_ready = sem("rows_ready")
        later_rows_ready = sem("later_rows_ready")
        weights_loaded = sem("weights_loaded")
        scan_loaded = sem("scan_loaded")
        head_loaded = sem("head_loaded")
        ones_ready = sem("ones_ready")
        zeros_ready = sem("zeros_ready")
        gathered = [[sem(f"gathered_{s}_{g}") for g in range(len(FULL))] for s in range(SLOTS)]
        turned = sem("turned")
        moved = sem("moved")
        multiplied = sem("multiplied")
        raw_ready = sem("raw_ready")
        rows_in = [sem(f"rows_in_{k}") for k in range(2)]
        loads_used = sem("loads_used")
        split_in = sem("split_in")
        split_step = sem("split_step")
        split_done = sem("split_done")
        ids_spread = sem("ids_spread")
        reach_step = sem("reach_step")
        mask_ready = sem("mask_ready")
        mask_used = sem("mask_used")
        picked_ready = sem("picked_ready")
        picked_moved = sem("picked_moved")
        y_ready = sem("y_ready")
        stored = sem("stored")

        block = ctx.enter_context(nc.Block())

        @block.sync
        def _(sp):
            sp.dma_start(pair_ids[:, 0, :], user_ids.rearrange("(p t) -> p t", p=P)).then_inc(pair_loaded, DMA_INC)
            sp.dma_start(eye[:], ident).then_inc(weights_loaded, DMA_INC)
            sp.dma_start(b1_row[:], b1.rearrange("(a n) -> a n", a=1)).then_inc(weights_loaded, DMA_INC)
            sp.dma_start(w1[:], W1.rearrange("(c p) n -> p c n", p=P)).then_inc(weights_loaded, DMA_INC)
            for a in range(SCANNED):
                table = sparse_tables[first_scanned_field + a].rearrange("(p r) e -> p (r e)", r=REACH)
                with sp.Fori(0, loads // (2 * SCANNED)) as r:
                    for k in range(2):
                        part = table[:, bass.ds(r * (2 * LOADED * cols) + k * LOADED * cols, LOADED * cols)]
                        sp.wait_ge(loads_used, r * 2 + (a * loads // SCANNED + k + 1))
                        sp.dma_start(loaded_rows[k][:SPREAD, :], part[:SPREAD]).then_inc(rows_in[k], DMA_INC)
                        sp.dma_start(loaded_rows[k][SPREAD:, :], part[SPREAD:]).then_inc(rows_in[k], DMA_INC)
            sp.wait_ge(y_ready, 1)
            sp.dma_start(out.rearrange("(p t) a -> p (t a)", p=P), y[:]).then_inc(stored, DMA_INC)
            sp.wait_ge(stored, DMA_INC)

        @block.gpsimd
        def _(pool):
            def gather_tile(i, s, groups, last_field):
                parts = [range(first * per_chunk, last * per_chunk) for first, last in groups]
                if last_field:
                    parts.append([fields + 1])
                for g, part in enumerate(parts):
                    for f in part:
                        if f in (0, 2):
                            pool.wait_ge(rows_ready, i * (2 * SLOTS) + (2 * s + 1 + f // 2))
                            pool.nop(nofuse=True)
                        table = (user_emb, item_emb)[f] if f < 2 else sparse_rows
                        nc.gpsimd.indirect_dma_start(
                            out=x[s][:, f * emb:(f + 1) * emb], out_offset=None, in_=table,
                            in_offset=bass.IndirectOffsetOnAxis(ap=rows[s][:, f:f + 1], axis=0),
                            element_offset=max(f - 2, 0) * sparse_vocab * emb,
                        ).then_inc(gathered[s][g], DMA_INC)

            with pool.Fori(0, FIRST_SCANNED) as i:
                for s in range(SLOTS):
                    gather_tile(i, s, FULL, False)
            with pool.Fori(FIRST_SCANNED, steps) as i:
                for s in range(SLOTS):
                    gather_tile(i, s, GATHERED, half(i, s))

        @block.vector
        def _(dve):
            def table_rows(ids, w, to, size, counter, n, done):
                nc.vector.tensor_scalar(w, ids, 0.0, float(size), ALU.is_lt, ALU.mult).then_inc(counter, 1)
                dve.wait_ge(counter, n + 1)
                nc.vector.tensor_tensor(w, w, ids, ALU.add).then_inc(counter, 1)
                dve.wait_ge(counter, n + 2)
                nc.vector.tensor_scalar(to, w, 0.0, float(size - 1), ALU.max, ALU.min).then_inc(done, 1)

            def head(i, s):
                dve.wait_ge(multiplied, group_base(i) + ((s + 1) * len(groups_of(i)) + AHEAD))
                dve.wait_ge(raw_ready, i * SLOTS + (s + AHEAD))
                nc.vector.scalar_tensor_tensor(
                    out=weighed[:], in0=h_ps[s][:, :hidden], scalar=0.0, in1=w2_all[:], op0=ALU.max,
                    op1=ALU.mult, accum_out=raw[:, bass.ds(i * SLOTS + s, 1)]).then_inc(raw_ready, 1)

            def reach(u):
                n = u * 5
                dve.wait_ge(ids_spread, u + 1)
                ids = spread_ps[:holders, :width]
                nc.vector.tensor_scalar(wanted[:], ids, 0.0, float(sparse_vocab), ALU.is_lt, ALU.mult).then_inc(reach_step, 1)
                dve.wait_ge(reach_step, n + 1)
                nc.vector.tensor_tensor(wanted[:], ids, wanted[:], ALU.add).then_inc(reach_step, 1)
                dve.wait_ge(reach_step, n + 2)
                nc.vector.tensor_scalar(wanted[:], wanted[:], 0.0, float(sparse_vocab - 1), ALU.max, ALU.min).then_inc(reach_step, 1)
                dve.wait_ge(reach_step, n + 3)
                nc.vector.tensor_scalar(reach_of[:], wanted[:], numbers[:holders, REACH:REACH + 1], None,
                                        ALU.subtract).then_inc(reach_step, 1)
                dve.wait_ge(reach_step, n + 4)
                nc.vector.tensor_copy(reach_words, reach_of[:].bitcast(U32)).then_inc(reach_step, 1)

            def masks(u):
                n = u * 5
                with dve.Fori(0, rounds) as j:
                    for k in range(MASKS):
                        if k == 0:
                            dve.wait_ge(reach_step, n + 5)
                        if k % AT_ONCE == 0:
                            dve.wait_ge(mask_used, u * REACH + (j * MASKS + (k + AT_ONCE)))
                        nc.vector.tensor_scalar(mask[k][:], reach_ps, numbers[:holders, bass.ds(j * MASKS + k, 1)], None,
                                                ALU.is_equal).then_inc(mask_ready, 1)

            dve.wait_ge(pair_loaded, 2 * DMA_INC)
            for s in range(SLOTS):
                if s == 1:
                    dve.wait_ge(rows_ready, 2)
                n = 4 * s
                table_rows(pair_ids[:, :, s], wrap[:, 0:2], rows[s][:, 0:2], vocab, index_step, n, rows_ready)
                if s == 0:
                    dve.wait_ge(fields_loaded, DMA_INC)
                table_rows(field_ids[:, s, :], wrap[:, 2:], rows[s][:, 2:], sparse_vocab, index_step, n + 2, rows_ready)
            table_rows(pair_ids[:, :, SLOTS:].rearrange("p f t -> p t f"), wrap_later[:, :, 0:2],
                       later_rows[:, :, 0:2], vocab, index_step, 4 * SLOTS, later_rows_ready)
            table_rows(field_ids[:, SLOTS:, :], wrap_later[:, :, 2:],
                       later_rows[:, :, 2:], sparse_vocab, index_step, 4 * SLOTS + 2, later_rows_ready)
            nc.vector.memset(ones_row[:], 1.0).then_inc(ones_ready, 1)
            dve.sem_inc(raw_ready, AHEAD)
            dve.sem_inc(split_done, AHEAD)
            nc.vector.memset(zeros[:].bitcast(U32), 0).then_inc(zeros_ready, 1)
            nc.vector.memset(low[:].bitcast(U32)[:, :, emb // 2:], 0).then_inc(zeros_ready, 1)

            with dve.Fori(0, pieces // 2) as r:
                for k in range(2):
                    here = bass.ds(r * (2 * PIECE) + k * PIECE, PIECE)
                    rest = split_ps[k][:holders, :cols].rearrange("p (r e) -> p r e", e=emb)
                    n = r * 4 + 2 * k
                    dve.wait_ge(split_in, r * 2 + (k + 1))
                    nc.vector.tensor_tensor(rest, rest, high_mid[:, here, :emb], ALU.subtract).then_inc(split_step, 1)
                    dve.wait_ge(split_step, n + 1)
                    nc.vector.tensor_copy(high_mid[:, here, emb:], rest).then_inc(split_step, 1)
                    dve.wait_ge(split_step, n + 2)
                    nc.vector.tensor_tensor(low[:, here, :emb], rest, high_mid[:, here, emb:], ALU.subtract).then_inc(split_done, 1)

            dve.wait_ge(head_loaded, 2 * DMA_INC)
            dve.wait_ge(scan_loaded, (2 * SCANNED + 1) * DMA_INC)
            for i in range(FIRST_SCANNED):
                reach(i)
                for s in range(SLOTS):
                    head(i, s)
                masks(i)
            with dve.Fori(FIRST_SCANNED, steps - 2) as i:
                reach(i)
                for s in range(SLOTS):
                    head(i, s)
                masks(i)
            for i in range(steps - 2, steps):
                for s in range(SLOTS):
                    head(i, s)

        @block.scalar
        def _(act):
            act.dma_start(pair_ids[:, 1, :], item_ids.rearrange("(p t) -> p t", p=P)).then_inc(pair_loaded, DMA_INC)
            act.dma_start(field_ids[:].rearrange("p t f -> p (t f)"),
                          sparse_ids.rearrange("(p t) f -> p (t f)", p=P)).then_inc(fields_loaded, DMA_INC)
            act.dma_start(scan_ids[:], scan_order_ids).then_inc(scan_ids_loaded, DMA_INC)
            act.dma_start(numbers[:], scan_numbers).then_inc(scan_loaded, DMA_INC)
            for a in range(SCANNED):
                w = W1[features - (SCANNED - a) * emb:features - (SCANNED - a - 1) * emb, :]
                act.dma_start(w1_scan[:emb, a, :], w).then_inc(scan_loaded, DMA_INC)
                act.dma_start(w1_scan[emb:, a, :], w).then_inc(scan_loaded, DMA_INC)
            act.dma_start(w2_all[:], W2.rearrange("n a -> a n").broadcast_to([P, hidden])).then_inc(head_loaded, DMA_INC)
            act.dma_start(b2_all[:], b2.rearrange("(a n) -> a n", a=1).broadcast_to([P, 1])).then_inc(head_loaded, DMA_INC)
            act.sem_inc(loads_used, AHEAD)
            nc.scalar.activation(warm[:], nc.const_aps.tensor(0.0, (1, 1), F32), ACT.Sigmoid)
            act.wait_ge(scan_ids_loaded, DMA_INC)
            nc.scalar.copy(scan_ids_f[:], scan_ids[:]).then_inc(scan_ids_ready, 1)

            def move(i, s, g):
                first, last = groups_of(i)[g]
                n = s * len(groups_of(i)) + g
                size = (last - first) * P
                act.wait_ge(turned, group_base(i) + (n + 1))
                act.wait_ge(multiplied, group_base(i) + (n + 1))
                if half(i, s) and g == len(GATHERED) - 1:
                    nc.scalar.copy(xt[n % 2][:emb, size:size + P], xt_ps[n % 2][:emb, size:size + P])
                nc.scalar.copy(xt[n % 2][:, :size], xt_ps[n % 2][:, :size]).then_inc(moved, 1)

            def next_rows(i, s):
                for first, last in ((0, 2), (2, fields + 2)):
                    nc.scalar.copy(rows[s][:, first:last], later_rows[:, bass.ds(i * SLOTS + s, 1), first:last]
                                   .rearrange("p t f -> p (t f)")).then_inc(rows_ready, 1)

            def split_piece(m):
                load, sub = m // LOADED, m % LOADED
                piece = loaded_rows[load % 2][:, sub * cols:(sub + 1) * cols].rearrange("p (r e) -> p r e", e=emb)
                act.wait_ge(rows_in[load % 2], (load // 2 + 1) * 2 * DMA_INC)
                nc.scalar.copy(high_mid[:, m * PIECE:(m + 1) * PIECE, :emb], piece)
                act.wait_ge(split_done, m + 1)
                nc.scalar.copy(split_ps[m % 2][:holders, :cols].rearrange("p (r e) -> p r e", e=emb),
                               piece).then_inc(split_in, 1)
                if sub == LOADED - 1:
                    act.wait_ge(split_in, m + 1)
                    act.sem_inc(loads_used, 1)

            def step(i, scan):
                for s in range(SLOTS):
                    for g in range(len(groups_of(i))):
                        move(i, s, g)
                        if isinstance(i, int) and i == 0:
                            for m in range(split_per_group):
                                split_piece((s * len(FULL) + g) * split_per_group + m)
                    if not (isinstance(i, int) and i == steps - 1):
                        next_rows(i, s)
                if scan is not None:
                    act.wait_ge(picked_ready, scan + 1)
                    nc.scalar.copy(picked[:], picked_ps[:, :width]).then_inc(picked_moved, 1)

            split_per_group = pieces // (SLOTS * len(FULL))
            act.wait_ge(later_rows_ready, 2)
            step(0, None)
            step(1, 0)
            with act.Fori(FIRST_SCANNED, steps - 1) as i:
                step(i, i - 1)
            step(steps - 1, None)
            act.wait_ge(head_loaded, 2 * DMA_INC)
            act.wait_ge(raw_ready, tiles + AHEAD)
            nc.scalar.activation(y[:], raw[:], ACT.Sigmoid, bias=b2_all[:, 0:1]).then_inc(y_ready, 1)

        @block.tensor
        def _(pe):
            def turn(i, s, g):
                first, last = groups_of(i)[g]
                n = s * len(groups_of(i)) + g
                count = (last - first) * per_chunk
                pe.wait_ge(gathered[s][g], i * (count * DMA_INC) + count * DMA_INC)
                if half(i, s) and g == len(GATHERED) - 1:
                    pe.wait_ge(gathered[s][g + 1], i * DMA_INC + (FIRST_SCANNED * (per_chunk - 1) + 1) * DMA_INC)
                for c in range(first, last):
                    mm = nc.tensor.transpose(xt_ps[n % 2][:, (c - first) * P:(c - first + 1) * P],
                                             x[s][:, c * P:(c + 1) * P], eye[:])
                if half(i, s) and g == len(GATHERED) - 1:
                    mm = nc.tensor.transpose(xt_ps[n % 2][:emb, (last - first) * P:(last - first + 1) * P],
                                             x[s][:, (fields + 1) * emb:], eye[:])
                mm.then_inc(turned, 1)

            def multiply(i, s, g):
                groups = groups_of(i)
                first, last = groups[g]
                n = s * len(groups) + g
                pe.wait_ge(moved, group_base(i) + (n + 1))
                for c in range(first, last):
                    mm = nc.tensor.matmul(h_ps[s][:, :hidden], xt[n % 2][:, (c - first) * P:(c - first + 1) * P],
                                          w1[:, c, :], start=False,
                                          stop=(c == groups[-1][1] - 1 and not half(i, s)))
                if half(i, s) and g == len(groups) - 1:
                    mm = nc.tensor.matmul(h_ps[s][:, :hidden], xt[n % 2][:emb, (last - first) * P:(last - first + 1) * P],
                                          w1_scan[:emb, SCANNED - 1, :], start=False, stop=True)
                mm.then_inc(multiplied, 1)

            def scan_rounds(u, start, count):
                with pe.Fori(start, start + count) as j:
                    for k in range(MASKS):
                        pe.wait_ge(mask_ready, u * REACH + (j * MASKS + (k + 1)))
                        for part in (high_mid, low):
                            for a, (at, size) in enumerate(table_cols):
                                mm = nc.tensor.matmul(
                                    picked_ps[:, at:at + size],
                                    part[:, bass.ds(j * MASKS + (a * REACH + k), 1), :].rearrange("p r e -> p (r e)"),
                                    mask[k][:, at:at + size], start=False, stop=False)
                        mm.then_inc(mask_used, 1)

            def spread_ids(u):
                nc.tensor.matmul(spread_ps[:, :width], ones_row[:], scan_ids_f[:, bass.ds(u * width, width)],
                                 start=True, stop=True).then_inc(ids_spread, 1)

            def step(i, u, add_picked, spread_next):
                done = 0
                for s in range(SLOTS):
                    turn(i, s, 0)
                    if s == 0 and add_picked:
                        pe.wait_ge(picked_moved, i - (FIRST_SCANNED - 1))
                    if s == 0 and u is not None:
                        nc.tensor.matmul(picked_ps[:, :width], zeros[:, :P], zeros[:], start=True, stop=False)
                    pe.wait_ge(raw_ready, i * SLOTS + (s + 1))
                    nc.tensor.matmul(h_ps[s][:, :hidden], ones_row[:], b1_row[:], start=True, stop=False)
                    if add_picked:
                        for a, at in block_cols[s]:
                            nc.tensor.matmul(h_ps[s][:, :hidden], picked[:, at:at + P],
                                             w1_scan[:, a, :], start=False, stop=False)
                    for g in range(len(groups_of(i))):
                        if g > 0:
                            turn(i, s, g)
                        if u is not None:
                            scan_rounds(u, done, rounds_after(i)[g])
                            done += rounds_after(i)[g]
                        multiply(i, s, g)
                    if s == 0 and spread_next is not None:
                        spread_ids(spread_next)
                if u is not None:
                    nc.tensor.matmul(picked_ps[:, :width], zeros[:, :P], zeros[:], start=False, stop=True).then_inc(picked_ready, 1)

            pe.wait_ge(weights_loaded, 3 * DMA_INC)
            pe.wait_ge(ones_ready, 1)
            pe.sem_inc(multiplied, AHEAD)
            pe.sem_inc(mask_used, MASKS)
            step(0, None, False, None)
            pe.wait_ge(scan_ids_ready, 1)
            pe.wait_ge(zeros_ready, 2)
            pe.wait_ge(scan_loaded, (2 * SCANNED + 1) * DMA_INC)
            pe.wait_ge(split_done, pieces + AHEAD)
            spread_ids(0)
            step(1, 0, False, 1)
            with pe.Fori(FIRST_SCANNED, steps - 2) as i:
                step(i, i - 1, True, i)
            step(steps - 2, steps - 3, True, None)
            step(steps - 1, None, True, None)


_INS = ['r_user_ids', 'r_item_ids', 'r_sparse_features', 'L0_rec_user_emb', 'L0_rec_item_emb',
        'L0_rec_sparse_tables', 'L0_rec_W1', 'L0_rec_b1', 'L0_rec_W2', 'L0_rec_b2']


def kernel(**inputs):
    import numpy as _np
    import concourse.bacc as _bacc
    from concourse import mybir as _mybir
    from concourse.bass_utils import run_bass_kernel_spmd as _run

    nc = _bacc.Bacc("TRN2", target_bir_lowering=False, num_devices=1)
    arrays, args = {}, []

    def give(name, a):
        arrays[name] = a
        args.append(nc.dram_tensor(name, a.shape, _mybir.dt.from_np(a.dtype), kind="ExternalInput").ap())

    for name in _INS:
        give(f"in_{name}_dram", _np.ascontiguousarray(inputs[name]))
    ids = arrays["in_r_sparse_features_dram"]
    tiles = ids.shape[0] // P
    ids = ids.reshape(P, tiles // SLOTS, SLOTS, -1)[:, FIRST_SCANNED:, :, -SCANNED:]
    ids = _np.stack([ids[:, :, slot, table] for table, slot in BLOCKS])
    give("scan_ids_dram", _np.ascontiguousarray(ids.transpose(2, 0, 1)).reshape(1, -1))
    give("eye_dram", _np.eye(P, dtype=_np.float32))
    numbers = _np.zeros((P, REACH + 1), _np.float32)
    numbers[:, :REACH] = _np.arange(REACH)
    numbers[:, REACH] = REACH * _np.arange(P)
    give("numbers_dram", numbers)
    args.append(nc.dram_tensor("out_dram", (2048, 1), _mybir.dt.float32, kind="ExternalOutput").ap())
    rec_mlp(nc, *args)
    r = _run(nc, [arrays], core_ids=[0])
    return r.results[0]["out_dram"]
```
